# Optimizing a Trainium2 kernel written in Bass

```python
import numpy as np
import jax
import jax.numpy as jnp

def _softmax(x, axis=-1):
    return jax.nn.softmax(x, axis=axis)
def _gelu(x):
    return jax.nn.gelu(x, approximate=True)
def _silu(x):
    return jax.nn.silu(x)
def _sigmoid(x):
    return jax.nn.sigmoid(x)
def _layernorm(x, axis=-1, eps=1e-5):
    m = jnp.mean(x, axis=axis, keepdims=True)
    v = jnp.var(x, axis=axis, keepdims=True)
    return (x - m) / jnp.sqrt(v + eps)
def _scatter_add(tgt, idx, src, axis=0):
    return tgt.at[idx].add(src)
def _segment_sum(src, seg, n):
    return jax.ops.segment_sum(src, seg, n)

kernel_name = 'mk_rec_standalone_d1_rec_4bbf2e'

def setup_inputs(seed: int = 0):
    np.random.seed(seed)
    _w = jnp.asarray
    def _rec_inputs():
        import jax
        import jax.numpy as jnp
        _rk = jax.random.key(seed)
        r_nodes = jax.random.randint(jax.random.fold_in(_rk, 1), (4096,), 72, 99964, jnp.int32)
        r_uv_adjacency = jnp.stack([jax.random.randint(jax.random.fold_in(jax.random.fold_in(_rk, 2), 0), (4096,), 8, 99996, jnp.int32), jax.random.randint(jax.random.fold_in(jax.random.fold_in(_rk, 2), 1), (4096,), 22, 99999, jnp.int32), jax.random.randint(jax.random.fold_in(jax.random.fold_in(_rk, 2), 2), (4096,), 0, 99998, jnp.int32), jax.random.randint(jax.random.fold_in(jax.random.fold_in(_rk, 2), 3), (4096,), 13, 99999, jnp.int32), jax.random.randint(jax.random.fold_in(jax.random.fold_in(_rk, 2), 4), (4096,), 2, 99999, jnp.int32), jax.random.randint(jax.random.fold_in(jax.random.fold_in(_rk, 2), 5), (4096,), 23, 100000, jnp.int32), jax.random.randint(jax.random.fold_in(jax.random.fold_in(_rk, 2), 6), (4096,), 2, 99992, jnp.int32), jax.random.randint(jax.random.fold_in(jax.random.fold_in(_rk, 2), 7), (4096,), 2, 99998, jnp.int32), jax.random.randint(jax.random.fold_in(jax.random.fold_in(_rk, 2), 8), (4096,), 0, 99979, jnp.int32), jax.random.randint(jax.random.fold_in(jax.random.fold_in(_rk, 2), 9), (4096,), 12, 99973, jnp.int32), jax.random.randint(jax.random.fold_in(jax.random.fold_in(_rk, 2), 10), (4096,), 10, 100000, jnp.int32), jax.random.randint(jax.random.fold_in(jax.random.fold_in(_rk, 2), 11), (4096,), 1, 99974, jnp.int32), jax.random.randint(jax.random.fold_in(jax.random.fold_in(_rk, 2), 12), (4096,), 14, 99991, jnp.int32), jax.random.randint(jax.random.fold_in(jax.random.fold_in(_rk, 2), 13), (4096,), 9, 99944, jnp.int32), jax.random.randint(jax.random.fold_in(jax.random.fold_in(_rk, 2), 14), (4096,), 29, 99992, jnp.int32), jax.random.randint(jax.random.fold_in(jax.random.fold_in(_rk, 2), 15), (4096,), 19, 99994, jnp.int32), jax.random.randint(jax.random.fold_in(jax.random.fold_in(_rk, 2), 16), (4096,), 37, 99984, jnp.int32), jax.random.randint(jax.random.fold_in(jax.random.fold_in(_rk, 2), 17), (4096,), 2, 99997, jnp.int32), jax.random.randint(jax.random.fold_in(jax.random.fold_in(_rk, 2), 18), (4096,), 14, 99998, jnp.int32), jax.random.randint(jax.random.fold_in(jax.random.fold_in(_rk, 2), 19), (4096,), 0, 99993, jnp.int32), jax.random.randint(jax.random.fold_in(jax.random.fold_in(_rk, 2), 20), (4096,), 0, 99993, jnp.int32), jax.random.randint(jax.random.fold_in(jax.random.fold_in(_rk, 2), 21), (4096,), 5, 99992, jnp.int32), jax.random.randint(jax.random.fold_in(jax.random.fold_in(_rk, 2), 22), (4096,), 6, 99998, jnp.int32), jax.random.randint(jax.random.fold_in(jax.random.fold_in(_rk, 2), 23), (4096,), 7, 99995, jnp.int32), jax.random.randint(jax.random.fold_in(jax.random.fold_in(_rk, 2), 24), (4096,), 0, 99986, jnp.int32), jax.random.randint(jax.random.fold_in(jax.random.fold_in(_rk, 2), 25), (4096,), 12, 99990, jnp.int32), jax.random.randint(jax.random.fold_in(jax.random.fold_in(_rk, 2), 26), (4096,), 22, 99996, jnp.int32), jax.random.randint(jax.random.fold_in(jax.random.fold_in(_rk, 2), 27), (4096,), 55, 99973, jnp.int32), jax.random.randint(jax.random.fold_in(jax.random.fold_in(_rk, 2), 28), (4096,), 32, 99977, jnp.int32), jax.random.randint(jax.random.fold_in(jax.random.fold_in(_rk, 2), 29), (4096,), 10, 99982, jnp.int32), jax.random.randint(jax.random.fold_in(jax.random.fold_in(_rk, 2), 30), (4096,), 0, 99985, jnp.int32), jax.random.randint(jax.random.fold_in(jax.random.fold_in(_rk, 2), 31), (4096,), 1, 99996, jnp.int32), jax.random.randint(jax.random.fold_in(jax.random.fold_in(_rk, 2), 32), (4096,), 4, 99987, jnp.int32), jax.random.randint(jax.random.fold_in(jax.random.fold_in(_rk, 2), 33), (4096,), 2, 99943, jnp.int32), jax.random.randint(jax.random.fold_in(jax.random.fold_in(_rk, 2), 34), (4096,), 2, 99999, jnp.int32), jax.random.randint(jax.random.fold_in(jax.random.fold_in(_rk, 2), 35), (4096,), 5, 99995, jnp.int32), jax.random.randint(jax.random.fold_in(jax.random.fold_in(_rk, 2), 36), (4096,), 7, 99997, jnp.int32), jax.random.randint(jax.random.fold_in(jax.random.fold_in(_rk, 2), 37), (4096,), 13, 99958, jnp.int32), jax.random.randint(jax.random.fold_in(jax.random.fold_in(_rk, 2), 38), (4096,), 6, 100000, jnp.int32), jax.random.randint(jax.random.fold_in(jax.random.fold_in(_rk, 2), 39), (4096,), 14, 99985, jnp.int32), jax.random.randint(jax.random.fold_in(jax.random.fold_in(_rk, 2), 40), (4096,), 8, 99997, jnp.int32), jax.random.randint(jax.random.fold_in(jax.random.fold_in(_rk, 2), 41), (4096,), 0, 100000, jnp.int32), jax.random.randint(jax.random.fold_in(jax.random.fold_in(_rk, 2), 42), (4096,), 11, 100000, jnp.int32), jax.random.randint(jax.random.fold_in(jax.random.fold_in(_rk, 2), 43), (4096,), 7, 99999, jnp.int32), jax.random.randint(jax.random.fold_in(jax.random.fold_in(_rk, 2), 44), (4096,), 2, 99966, jnp.int32), jax.random.randint(jax.random.fold_in(jax.random.fold_in(_rk, 2), 45), (4096,), 5, 99986, jnp.int32), jax.random.randint(jax.random.fold_in(jax.random.fold_in(_rk, 2), 46), (4096,), 17, 99995, jnp.int32), jax.random.randint(jax.random.fold_in(jax.random.fold_in(_rk, 2), 47), (4096,), 28, 99989, jnp.int32), jax.random.randint(jax.random.fold_in(jax.random.fold_in(_rk, 2), 48), (4096,), 6, 100000, jnp.int32), jax.random.randint(jax.random.fold_in(jax.random.fold_in(_rk, 2), 49), (4096,), 15, 99963, jnp.int32), jax.random.randint(jax.random.fold_in(jax.random.fold_in(_rk, 2), 50), (4096,), 4, 99991, jnp.int32), jax.random.randint(jax.random.fold_in(jax.random.fold_in(_rk, 2), 51), (4096,), 2, 99960, jnp.int32), jax.random.randint(jax.random.fold_in(jax.random.fold_in(_rk, 2), 52), (4096,), 2, 99996, jnp.int32), jax.random.randint(jax.random.fold_in(jax.random.fold_in(_rk, 2), 53), (4096,), 5, 99999, jnp.int32), jax.random.randint(jax.random.fold_in(jax.random.fold_in(_rk, 2), 54), (4096,), 23, 99993, jnp.int32), jax.random.randint(jax.random.fold_in(jax.random.fold_in(_rk, 2), 55), (4096,), 2, 99970, jnp.int32), jax.random.randint(jax.random.fold_in(jax.random.fold_in(_rk, 2), 56), (4096,), 8, 99988, jnp.int32), jax.random.randint(jax.random.fold_in(jax.random.fold_in(_rk, 2), 57), (4096,), 0, 99986, jnp.int32), jax.random.randint(jax.random.fold_in(jax.random.fold_in(_rk, 2), 58), (4096,), 8, 99993, jnp.int32), jax.random.randint(jax.random.fold_in(jax.random.fold_in(_rk, 2), 59), (4096,), 3, 99998, jnp.int32), jax.random.randint(jax.random.fold_in(jax.random.fold_in(_rk, 2), 60), (4096,), 5, 99994, jnp.int32), jax.random.randint(jax.random.fold_in(jax.random.fold_in(_rk, 2), 61), (4096,), 8, 99999, jnp.int32), jax.random.randint(jax.random.fold_in(jax.random.fold_in(_rk, 2), 62), (4096,), 1, 99996, jnp.int32), jax.random.randint(jax.random.fold_in(jax.random.fold_in(_rk, 2), 63), (4096,), 32, 99990, jnp.int32)], axis=1)
        r_ratings = jax.random.randint(jax.random.fold_in(_rk, 3), (4096, 64), 0, 5, jnp.int32)
        return r_nodes, r_uv_adjacency, r_ratings
    r_nodes, r_uv_adjacency, r_ratings = _rec_inputs()
    def _L0_rec_setup():
        import jax, jax.numpy as jnp
        import numpy as np
        N, DEG, D = (8192, 64, 128)
        NUM_USERS, NUM_ITEMS, NUM_RATINGS = (100000, 100000, 5)
        key = jax.random.key(seed)
        ks = jax.random.split(key, 16)
        s = 0.05
        inp = {'nodes': jax.random.randint(ks[0], (N,), 0, NUM_USERS), 'uv_adjacency': jax.random.randint(ks[1], (N, DEG), 0, NUM_ITEMS), 'ratings': jax.random.randint(ks[2], (N, DEG), 0, NUM_RATINGS), 'user_emb': jax.random.normal(ks[3], (NUM_USERS, D), jnp.float32) * s, 'item_emb': jax.random.normal(ks[4], (NUM_ITEMS, D), jnp.float32) * s, 'rating_emb': jax.random.normal(ks[5], (NUM_RATINGS, D), jnp.float32) * s, 'w1': jax.random.normal(ks[6], (2 * D, D), jnp.float32) * s, 'b1': jnp.zeros((D,), jnp.float32), 'w2': jax.random.normal(ks[7], (D, D), jnp.float32) * s, 'b2': jnp.zeros((D,), jnp.float32), 'wa1': jax.random.normal(ks[8], (2 * D, D), jnp.float32) * s, 'ba1': jnp.zeros((D,), jnp.float32), 'wa2': jax.random.normal(ks[9], (D, D), jnp.float32) * s, 'ba2': jnp.zeros((D,), jnp.float32), 'wa3': jax.random.normal(ks[10], (D, 1), jnp.float32) * s, 'ba3': jnp.zeros((1,), jnp.float32)}
        return inp
    _L0_rec_all = _L0_rec_setup()
    _L0_rec_in = {k: v for k, v in _L0_rec_all.items() if k in ('user_emb', 'item_emb', 'rating_emb', 'w1', 'b1', 'w2', 'b2', 'wa1', 'ba1', 'wa2', 'ba2', 'wa3', 'ba3', )}
    del _L0_rec_all

    return {
        "r_nodes": r_nodes,
        "r_uv_adjacency": r_uv_adjacency,
        "r_ratings": r_ratings,
        "L0_rec_user_emb": _L0_rec_in["user_emb"],
        "L0_rec_item_emb": _L0_rec_in["item_emb"],
        "L0_rec_rating_emb": _L0_rec_in["rating_emb"],
        "L0_rec_w1": _L0_rec_in["w1"],
        "L0_rec_b1": _L0_rec_in["b1"],
        "L0_rec_w2": _L0_rec_in["w2"],
        "L0_rec_b2": _L0_rec_in["b2"],
        "L0_rec_wa1": _L0_rec_in["wa1"],
        "L0_rec_ba1": _L0_rec_in["ba1"],
        "L0_rec_wa2": _L0_rec_in["wa2"],
        "L0_rec_ba2": _L0_rec_in["ba2"],
        "L0_rec_wa3": _L0_rec_in["wa3"],
        "L0_rec_ba3": _L0_rec_in["ba3"],
    }

def reference(r_nodes, r_uv_adjacency, r_ratings, L0_rec_user_emb, L0_rec_item_emb, L0_rec_rating_emb, L0_rec_w1, L0_rec_b1, L0_rec_w2, L0_rec_b2, L0_rec_wa1, L0_rec_ba1, L0_rec_wa2, L0_rec_ba2, L0_rec_wa3, L0_rec_ba3):
    import jax
    import jax.numpy as jnp
    def _L0_rec_ref(nodes, uv_adjacency, ratings, user_emb, item_emb, rating_emb, w1, b1, w2, b2, wa1, ba1, wa2, ba2, wa3, ba3):
        import jax, jax.numpy as jnp
        import numpy as np
        N, DEG, D = (8192, 64, 128)
        NUM_USERS, NUM_ITEMS, NUM_RATINGS = (100000, 100000, 5)
        e = item_emb[uv_adjacency]
        r = rating_emb[ratings]
        p = user_emb[nodes]
        x = jax.nn.relu(jnp.concatenate([e, r], axis=-1) @ w1 + b1)
        x = jax.nn.relu(x @ w2 + b2)
        pb = jnp.broadcast_to(p[:, None, :], x.shape)
        a = jax.nn.relu(jnp.concatenate([x, pb], axis=-1) @ wa1 + ba1)
        a = jax.nn.relu(a @ wa2 + ba2)
        logits = (a @ wa3 + ba3)[..., 0]
        attn = jax.nn.softmax(logits, axis=-1)
        return jnp.einsum('nk,nkd->nd', attn, x)

    y = _L0_rec_ref(r_nodes, r_uv_adjacency, r_ratings, L0_rec_user_emb, L0_rec_item_emb, L0_rec_rating_emb, L0_rec_w1, L0_rec_b1, L0_rec_w2, L0_rec_b2, L0_rec_wa1, L0_rec_ba1, L0_rec_wa2, L0_rec_ba2, L0_rec_wa3, L0_rec_ba3)
    return y


_drawn_inputs = setup_inputs


def setup_inputs(seed=0):
    import zlib

    import numpy as np

    out = dict(_drawn_inputs(seed))
    spreads = {'L0_rec_b1': (0.0, 0.1),
     'L0_rec_b2': (0.0, 0.1),
     'L0_rec_ba1': (0.0, 0.8),
     'L0_rec_ba2': (0.0, 0.8)}
    factors = {'L0_rec_user_emb': 8.0,
     'L0_rec_item_emb': 4.443,
     'L0_rec_wa1': 8.0,
     'L0_rec_wa2': 8.0,
     'L0_rec_wa3': 8.0}
    for name, (base, spread) in spreads.items():
        noise = np.random.default_rng([zlib.crc32(name.encode()), seed]).standard_normal(out[name].shape)
        drawn = base * np.exp(spread * noise) if base else spread * noise
        out[name] = jnp.asarray(drawn.astype(out[name].dtype))
    for name, factor in factors.items():
        out[name] = (out[name] * factor).astype(out[name].dtype)
    return out
```

```python
from contextlib import ExitStack

import concourse.bass as bass
import concourse.mybir as mybir
from concourse.alu_op_type import AluOpType as ALU
import numpy as np

F32 = mybir.dt.float32
F32R = mybir.dt.float32r
I32 = mybir.dt.int32
ACT = mybir.ActivationFunctionType
AX = mybir.AxisListType

P = 128
D = 128
NODES = 4096
DEG = 64
RATINGS = 5
TILE = 512
NPT = TILE // DEG
CPT = TILE // P
GT = 16
GN = GT * NPT
TILES = NODES // NPT
GROUPS = TILES // GT
QT = 4
GQ = GT // QT
HT = 8

LAG_L1, LAG_L2, LAG_A1, LAG_A2 = 1, 2, 3, 4
LAG_BC = 24
LAG_SUM = 25
LOGIT_DELAY = 2 * QT
R_PT, R_PCOPY, R_PW, R_PX = 8, 8, 10, 11
R_USER0, R_USER1 = 12, 4
R_MAX, R_SUB, R_EXPSUM, R_NORM, R_ATTN = 4, 5, 6, 7, 8
R_OUT = 9

FIRST = 3
GATHER_SLOTS = 8
X2_SLOTS = 32
A2_SLOTS = 8
DUP = 16

C_IDENT, C_SEL, C_RATING, C_LO, C_SGN, C_QUAD = 0, 128, 144, 145, 148, 151
C_WIDTH = 155


def constants():
    c = np.zeros((P, C_WIDTH), np.float32)
    c[:, C_IDENT:C_IDENT + P] = np.eye(P)
    p = np.arange(P)
    row = p % 32
    for t in range(GT):
        c[:, C_SEL + t] = (p // 32 == t % QT) & (row % DUP == t // QT)
    c[:, C_RATING] = np.where(row < 2 * RATINGS, row % RATINGS, -1)
    low = [row >= RATINGS, p % 16 >= NPT, row >= DUP]
    for k in range(3):
        c[:, C_LO + k] = low[k]
        c[:, C_SGN + k] = 1 - 2 * c[:, C_LO + k]
    for q in range(QT):
        c[:, C_QUAD + q] = p // 32 == q
    ind = np.zeros((P, HT, TILE), np.float32)
    for t in range(HT):
        ind[:, t] = (p[:, None] // 16 == t) & (p[:, None] % NPT == np.arange(TILE)[None] // DEG)
    return c, ind


def build_program(nc, edge_idx, node_idx, ratings, user_emb, item_emb, rating_emb, w1, b1, w2, b2,
                  wa1, ba1, wa2, ba2, wa3, ba3, consts, node_of_edge, out):
    ctx = ExitStack()
    with ctx:
        def sb(name, shape, dt=F32):
            return ctx.enter_context(nc.sbuf_tensor(name, shape, dt))

        def ps(name):
            return ctx.enter_context(nc.psum_tensor(name, [P, TILE], F32))

        def sem(name):
            return ctx.enter_context(nc.semaphore(name))

        cst = sb("cst", [P, C_WIDTH])
        ident = cst[:, C_IDENT:C_IDENT + P]
        gathered = sb("gathered", [P, GATHER_SLOTS, CPT, D])
        ind = sb("ind", [P, HT, TILE], F32R)
        sel = sb("sel", [P, GT, P], F32R)
        w1_f, w2_f = sb("w1_f", [P, 2, D]), sb("w2_f", [P, D])
        wa1_f, wa2_f = sb("wa1_f", [P, 2, D]), sb("wa2_f", [P, D])
        w1_hi, w1_lo = sb("w1_hi", [P, D], F32R), sb("w1_lo", [P, D], F32R)
        w2_hi, w2_lo = sb("w2_hi", [P, D], F32R), sb("w2_lo", [P, D], F32R)
        wa1_hi, wa1_lo = sb("wa1_hi", [P, D], F32R), sb("wa1_lo", [P, D], F32R)
        wa2_hi, wa2_lo = sb("wa2_hi", [P, D], F32R), sb("wa2_lo", [P, D], F32R)
        wa3_cols = sb("wa3_cols", [P, GQ, 32])
        wa3_f = sb("wa3_f", [P, 1])
        b2_col, ba2_col = sb("b2_col", [P, 1]), sb("ba2_col", [P, 1])
        b1_all, ba1_all = sb("b1_all", [P, D]), sb("ba1_all", [P, D])
        ba3_all = sb("ba3_all", [P, 1])
        rating_rows = sb("rating_rows", [P, D])
        rating_T = sb("rating_T", [P, P])
        rating_x = sb("rating_x", [P, D])
        rating_s = sb("rating_s", [P, D], F32R)
        rating_w = sb("rating_w", [P, D])
        rating_st = sb("rating_st", [P, QT, D], F32R)
        e_hi, e_lo = sb("e_hi", [P, 2, TILE], F32R), sb("e_lo", [P, 2, TILE], F32R)
        x1_hi, x1_lo = sb("x1_hi", [P, 2, TILE], F32R), sb("x1_lo", [P, 2, TILE], F32R)
        x2_hi, x2_lo = sb("x2_hi", [P, 2, TILE], F32R), sb("x2_lo", [P, 2, TILE], F32R)
        a1_hi, a1_lo = sb("a1_hi", [P, 2, TILE], F32R), sb("a1_lo", [P, 2, TILE], F32R)
        x2 = sb("x2", [P, X2_SLOTS * TILE])
        ind_f = x2[:, 0:HT * TILE].rearrange("p (t n) -> p t n", t=HT)
        a2 = sb("a2", [P, A2_SLOTS, TILE])
        rate_raw = sb("rate_raw", [P, GQ, TILE], I32)
        onehot = sb("onehot", [P, 2, TILE], F32R)
        idx = sb("idx", [P, GQ, QT * CPT], I32)
        nidx = sb("nidx", [P, 1], I32)
        user_rows = sb("user_rows", [P, D])
        user_T = sb("user_T", [P, GT, 2, NPT])
        user_x = sb("user_x", [P, 2, D])
        user_s = sb("user_s", [P, 2, D], F32R)
        user_st = sb("user_st", [P, 2, D], F32R)
        mx, mxb = sb("mx", [P, NPT]), sb("mxb", [P, NPT])
        den, rden = sb("den", [P, NPT]), sb("rden", [P, NPT])
        shifted = sb("shifted", [P, TILE])
        expo = sb("expo", [P, TILE])
        attn = shifted
        attn_s = sb("attn_s", [P, TILE], F32R)
        attn_w = sb("attn_w", [P, TILE], F32R)
        weighted = sb("weighted", [P, TILE])
        out_T = sb("out_T", [P, GN])
        out_rows = sb("out_rows", [P, D])

        ps_t, ps_l1, ps_l2, ps_a1 = ps("ps_t"), ps("ps_l1"), ps("ps_l2"), ps("ps_a1")
        ps_a2, ps_bc, ps_lg, ps_m = ps("ps_a2"), ps("ps_bc"), ps("ps_lg"), ps("ps_m")
        ps_out = ps_m[:, 0:P]
        ps_ut = ps_m[:, P:2 * P]
        ps_uw = ps_m[:, 2 * P:4 * P]

        s_const, s_const2 = sem("s_const"), sem("s_const2")
        s_zero, s_rrows = sem("s_zero"), sem("s_rrows")
        s_setup, s_rt, s_rtc, s_rw = sem("s_setup"), sem("s_rt"), sem("s_rtc"), sem("s_rw")
        s_dve = sem("s_dve")
        s_gather = [sem(f"s_gather{k}") for k in range(GATHER_SLOTS)]
        s_idx = [sem(f"s_idx{k}") for k in range(GQ)]
        s_rate = [sem(f"s_rate{k}") for k in range(GQ)]
        s_nidx, s_user = sem("s_nidx"), sem("s_user")
        s_t, s_l1, s_l2 = sem("s_t"), sem("s_l1"), sem("s_l2")
        s_a1, s_a2, s_bc = sem("s_a1"), sem("s_a2"), sem("s_bc")
        s_lg = sem("s_lg")
        s_e_hi, s_x1_hi, s_x2 = sem("s_e_hi"), sem("s_x1_hi"), sem("s_x2")
        s_x2_hi, s_a1_hi, s_a2f = sem("s_x2_hi"), sem("s_a1_hi"), sem("s_a2f")
        s_e_lo, s_x1_lo, s_x2_lo = sem("s_e_lo"), sem("s_x1_lo"), sem("s_x2_lo")
        s_a1_lo, s_mul, s_sum = sem("s_a1_lo"), sem("s_mul"), sem("s_sum")
        s_onehot = sem("s_onehot")
        s_ut, s_utc, s_uw = sem("s_ut"), sem("s_utc"), sem("s_uw")
        s_ux, s_us, s_ust = sem("s_ux"), sem("s_us"), sem("s_ust")
        s_max, s_maxb, s_sub, s_exp = sem("s_max"), sem("s_maxb"), sem("s_sub"), sem("s_exp")
        s_den, s_rden = sem("s_den"), sem("s_rden")
        s_attn, s_attn_s, s_attn_w = sem("s_attn"), sem("s_attn_s"), sem("s_attn_w")
        s_out_t, s_out_c, s_out = sem("s_out_t"), sem("s_out_c"), sem("s_out")

        block = ctx.enter_context(nc.Block())

        def live(g, r, lag):
            return not isinstance(g, int) or 0 <= GT * g + r - lag < TILES

        def done(g, r, lag):
            return g * GT + (r - lag + 1)

        def group_live(g, before):
            return not isinstance(g, int) or 0 <= g - before < GROUPS

        def groups(eng, group, last_rounds):
            for g in range(FIRST):
                group(g, GT)
            with eng.Fori(FIRST, GROUPS - 2) as g:
                group(g, GT)
            group(GROUPS - 2, GT)
            group(GROUPS - 1, GT)
            if last_rounds:
                group(GROUPS, GT)
                group(GROUPS + 1, last_rounds)

        @block.sync
        def _(sp):
            def load_quad(g, q):
                sp.dma_start(idx[:, q, :], edge_idx[g, q]).then_inc(s_idx[q], 16)
                for quad in range(QT):
                    sp.dma_start(rate_raw[32 * quad:32 * quad + 2 * RATINGS, q, :],
                                 ratings[g, q, quad].partition_broadcast(2 * RATINGS)
                                 ).then_inc(s_rate[q], 16)

            sp.dma_start(nidx[:], node_idx[0]).then_inc(s_nidx, 16)
            sp.dma_start(idx[:, 0, :], edge_idx[0, 0]).then_inc(s_idx[0], 16)
            for dst, src in (
                (cst[:], consts), (w1_f[:], w1.rearrange("(c p) n -> p c n", c=2)),
                (w2_f[:], w2), (wa1_f[:], wa1.rearrange("(c p) n -> p c n", c=2)),
                (wa2_f[:], wa2), (wa3_f[:], wa3),
                (b2_col[:], b2.rearrange("(p a) -> p a", a=1)),
                (ba2_col[:], ba2.rearrange("(p a) -> p a", a=1)),
                (b1_all[:], b1.partition_broadcast(P)), (ba1_all[:], ba1.partition_broadcast(P)),
                (ba3_all[:], ba3.partition_broadcast(P)),
            ):
                sp.dma_start(dst, src).then_inc(s_const, 16)
            sp.dma_start(ind_f, node_of_edge).then_inc(s_const2, 16)
            sp.wait_ge(s_zero, 1)
            for quad in range(QT):
                for part in range(2):
                    at = 32 * quad + RATINGS * part
                    sp.dma_start(rating_rows[at:at + RATINGS, :], rating_emb).then_inc(s_rrows, 16)
            for quad in range(QT):
                sp.dma_start(rate_raw[32 * quad:32 * quad + 2 * RATINGS, 0, :],
                             ratings[0, 0, quad].partition_broadcast(2 * RATINGS)
                             ).then_inc(s_rate[0], 16)
            for q in range(1, GQ):
                load_quad(0, q)

            def group(g, _):
                more = group_live(g, -1)
                for q in range(GQ):
                    if group_live(g, 0) and more:
                        sp.wait_ge(s_t, done(g, QT * q + QT - 1, 0))
                        load_quad(g + 1, q)
                    if q == 2 and group_live(g, 0) and group_live(g, -2):
                        sp.wait_ge(s_ut, g + 2)
                        sp.dma_start(nidx[:], node_idx[g + 2]).then_inc(s_nidx, 16)
                    if q == 3 and group_live(g, 2):
                        sp.wait_ge(s_out_c, g - 1)
                        sp.dma_start(out[g - 2], out_rows[:]).then_inc(s_out, 16)

            sp.wait_ge(s_ut, 1)
            sp.dma_start(nidx[:], node_idx[1]).then_inc(s_nidx, 16)
            groups(sp, group, GT)
            sp.wait_ge(s_out, 16 * GROUPS)

        @block.gpsimd
        def _(pool):
            def gather(dst, table, index):
                return nc.gpsimd.indirect_dma_start(
                    out=dst, out_offset=None, in_=table,
                    in_offset=bass.IndirectOffsetOnAxis(ap=index, axis=0))

            freed, users = pool.alloc_register("freed"), pool.alloc_register("users")
            pool.reg_mov(freed, done(FIRST, 0, GATHER_SLOTS))
            pool.reg_mov(users, (FIRST + 2) * 16)

            def wait_counted(semaphore, counted, by, g, value):
                if isinstance(g, int):
                    pool.wait_ge(semaphore, value)
                else:
                    pool.wait_ge(semaphore, counted)
                    pool.reg_add(counted, counted, by)

            pool.wait_ge(s_nidx, 16)
            gather(user_rows[:], user_emb, nidx[:, 0:1]).then_inc(s_user, 16)

            def group(g, rounds):
                for r in range(rounds):
                    if r % QT == 0:
                        pool.wait_ge(s_idx[r // QT], (g + 1) * 16)
                    slot = r % GATHER_SLOTS
                    if live(g, r, GATHER_SLOTS):
                        wait_counted(s_t, freed, 1, g, done(g, r, GATHER_SLOTS))
                    for c in range(CPT):
                        col = (r % QT) * CPT + c
                        gather(gathered[:, slot, c, :], item_emb,
                               idx[:, r // QT, col:col + 1]).then_inc(s_gather[slot], 16)
                    if r == 4 and group_live(g, -1):
                        wait_counted(s_nidx, users, 16, g, (g + 2) * 16)
                        gather(user_rows[:], user_emb, nidx[:, 0:1]).then_inc(s_user, 16)

            groups(pool, group, 0)

        @block.scalar
        def _(act):
            def copy_user():
                for dup in range(2):
                    step = nc.scalar.copy(user_T[:, :, dup, :],
                                          ps_ut.rearrange("p (t j) -> p t j", j=NPT))
                step.then_inc(s_utc, 1)

            act.wait_ge(s_rt, 1)
            nc.scalar.copy(rating_T[:], ps_m[:, 0:P]).then_inc(s_rtc, 1)
            act.wait_ge(s_ut, 1)
            copy_user()

            def group(g, rounds):
                for r in range(rounds):
                    if live(g, r, 0):
                        act.wait_ge(s_t, done(g, r, 0))
                        nc.scalar.activation(e_hi[:, r % 2, :], ps_t[:], ACT.Copy
                                             ).then_inc(s_e_hi, 1)
                    if live(g, r, LAG_L1):
                        act.wait_ge(s_l1, done(g, r, LAG_L1))
                        nc.scalar.activation(x1_hi[:, (r - LAG_L1) % 2, :], ps_l1[:], ACT.Relu
                                             ).then_inc(s_x1_hi, 1)
                    if live(g, r, LAG_L2):
                        act.wait_ge(s_l2, done(g, r, LAG_L2))
                        if isinstance(g, int):
                            at = (GT * g + r - LAG_L2) % X2_SLOTS * TILE
                        elif r >= LAG_L2:
                            at = (g % 2) * (GT * TILE) + (r - LAG_L2) * TILE
                        else:
                            at = ((g + 1) % 2) * (GT * TILE) + (GT + r - LAG_L2) * TILE
                        nc.scalar.activation(x2[:, bass.ds(at, TILE)], ps_l2[:], ACT.Relu,
                                             bias=b2_col[:, 0:1]).then_inc(s_x2, 1)
                        nc.scalar.activation(x2_hi[:, (r - LAG_L2) % 2, :], ps_l2[:], ACT.Relu,
                                             bias=b2_col[:, 0:1]).then_inc(s_x2_hi, 1)
                    if live(g, r, LAG_A1):
                        act.wait_ge(s_a1, done(g, r, LAG_A1))
                        nc.scalar.activation(a1_hi[:, (r - LAG_A1) % 2, :], ps_a1[:], ACT.Relu
                                             ).then_inc(s_a1_hi, 1)
                    if live(g, r, LAG_A2):
                        act.wait_ge(s_a2, done(g, r, LAG_A2))
                        nc.scalar.activation(a2[:, (r - LAG_A2) % A2_SLOTS, :], ps_a2[:], ACT.Relu,
                                             bias=ba2_col[:, 0:1]).then_inc(s_a2f, 1)
                    if r == R_SUB and group_live(g, 1):
                        act.wait_ge(s_sub, g)
                        nc.scalar.activation(expo[:], shifted[:], ACT.Exp).then_inc(s_exp, 1)
                    if r == R_PCOPY and group_live(g, 0) and group_live(g, -1):
                        act.wait_ge(s_ut, g + 2)
                        copy_user()
                    if r == R_OUT and group_live(g, 2):
                        act.wait_ge(s_out_t, g - 1)
                        if group_live(g, 3):
                            act.wait_ge(s_out, (g - 2) * 16)
                        nc.scalar.copy(out_rows[:], ps_out).then_inc(s_out_c, 1)

            groups(act, group, R_OUT + 1)

        @block.vector
        def _(dve):
            n = 0

            def step(ins):
                nonlocal n
                n += 1
                ins.then_inc(s_dve, 1)
                dve.wait_ge(s_dve, n)

            def split(hi, lo, whole):
                step(nc.vector.tensor_copy(hi, whole))
                step(nc.vector.tensor_tensor(lo, whole, hi, ALU.subtract))

            step(nc.vector.memset(rate_raw[:], 0))
            step(nc.vector.memset(wa3_cols[:], 0.0))
            nc.vector.memset(rating_rows[:], 0.0).then_inc(s_zero, 1)
            dve.wait_ge(s_const, 16 * 11)
            split(w1_hi[:], w1_lo[:], w1_f[:, 0, :])
            split(w2_hi[:], w2_lo[:], w2_f[:])
            split(wa1_hi[:], wa1_lo[:], wa1_f[:, 0, :])
            split(wa2_hi[:], wa2_lo[:], wa2_f[:])
            for j in range(GQ):
                for dup in range(2):
                    at = j + DUP * dup
                    step(nc.vector.tensor_copy(wa3_cols[:, j, at:at + 1], wa3_f[:]))
            for t in range(GT):
                step(nc.vector.tensor_copy(
                    sel[:, t, :], cst[:, C_SEL + t:C_SEL + t + 1].broadcast_to([P, P])))
            dve.wait_ge(s_const2, 16)
            step(nc.vector.tensor_copy(ind[:], ind_f))
            dve.wait_ge(s_rw, 1)
            step(nc.vector.tensor_tensor(rating_x[:], ps_m[:, P:2 * P], b1_all[:], ALU.add))
            step(nc.vector.tensor_scalar(rating_s[:], rating_x[:], cst[:, C_SGN:C_SGN + 1], None,
                                         ALU.mult))
            step(nc.vector.scalar_tensor_tensor(rating_w[:], rating_x[:], cst[:, C_LO:C_LO + 1],
                                                rating_s[:], ALU.mult, ALU.add))
            for q in range(QT):
                last = nc.vector.tensor_scalar(rating_st[:, q, :], rating_w[:],
                                               cst[:, C_QUAD + q:C_QUAD + q + 1], None, ALU.mult)
            last.then_inc(s_setup, 1)

            def make_onehot(g, q, more):
                dve.wait_ge(s_rate[q], (g + 1) * 16 * QT)
                nc.vector.tensor_scalar(onehot[:, q % 2, :], rate_raw[:, q, :],
                                        cst[:, C_RATING:C_RATING + 1], None, ALU.is_equal
                                        ).then_inc(s_onehot, 1)

            def user_split(g):
                dve.wait_ge(s_uw, g + 1)
                nc.vector.tensor_tensor(
                    user_x[:], ps_uw.rearrange("p (h d) -> p h d", h=2),
                    ba1_all[:].rearrange("p (a d) -> p a d", a=1).broadcast_to([P, 2, D]), ALU.add
                ).then_inc(s_ux, 1)
                dve.wait_ge(s_ux, g + 1)
                nc.vector.tensor_scalar(user_s[:], user_x[:], cst[:, C_SGN + 1:C_SGN + 2], None,
                                        ALU.mult).then_inc(s_us, 1)

            def user_join(g, half):
                dve.wait_ge(s_us, g + 1)
                nc.vector.scalar_tensor_tensor(
                    user_st[:, half, :], user_x[:, half, :], cst[:, C_LO + 1:C_LO + 2],
                    user_s[:, half, :], ALU.mult, ALU.add).then_inc(s_ust, 1)

            user_split(0)
            user_join(0, 0)
            user_join(0, 1)
            make_onehot(0, 0, True)

            def group(g, rounds):
                for r in range(rounds):
                    has_next = group_live(g, 0) and group_live(g, -1)
                    if live(g, r, 0):
                        dve.wait_ge(s_e_hi, done(g, r, 0))
                        nc.vector.tensor_tensor(e_lo[:, r % 2, :], ps_t[:], e_hi[:, r % 2, :],
                                                ALU.subtract).then_inc(s_e_lo, 1)
                    if live(g, r, LAG_SUM):
                        dve.wait_ge(s_bc, done(g, r, LAG_SUM))
                        if live(g, r, LAG_SUM + 1):
                            dve.wait_ge(s_sum, done(g, r, LAG_SUM + 1))
                        if isinstance(g, int):
                            at = (GT * g + r - LAG_SUM) % X2_SLOTS * TILE
                        elif r >= LAG_SUM - GT:
                            at = ((g + 1) % 2) * (GT * TILE) + (GT + r - LAG_SUM) * TILE
                        else:
                            at = (g % 2) * (GT * TILE) + (2 * GT + r - LAG_SUM) * TILE
                        nc.vector.tensor_tensor(weighted[:], ps_bc[:], x2[:, bass.ds(at, TILE)],
                                                ALU.mult).then_inc(s_mul, 1)
                    if r == R_ATTN and group_live(g, 1):
                        dve.wait_ge(s_attn_s, g)
                        nc.vector.scalar_tensor_tensor(
                            attn_w[:], attn[:], cst[:, C_LO + 2:C_LO + 3], attn_s[:],
                            ALU.mult, ALU.add).then_inc(s_attn_w, 1)
                    if live(g, r, LAG_L1):
                        dve.wait_ge(s_x1_hi, done(g, r, LAG_L1))
                        k = (r - LAG_L1) % 2
                        nc.vector.scalar_tensor_tensor(x1_lo[:, k, :], ps_l1[:], 0.0,
                                                       x1_hi[:, k, :], ALU.max, ALU.subtract
                                                       ).then_inc(s_x1_lo, 1)
                    if live(g, r, LAG_SUM):
                        dve.wait_ge(s_mul, done(g, r, LAG_SUM))
                        if r == R_OUT and group_live(g, 2):
                            dve.wait_ge(s_out_t, g - 1)
                        t = (r - LAG_SUM) % GT
                        nc.vector.reduce_sum(
                            out_T[:, NPT * t:NPT * t + NPT],
                            weighted[:].rearrange("p (n k) -> p n k", k=DEG), axis=AX.X
                        ).then_inc(s_sum, 1)
                    if live(g, r, LAG_L2):
                        dve.wait_ge(s_x2_hi, done(g, r, LAG_L2))
                        k = (r - LAG_L2) % 2
                        if isinstance(g, int):
                            at = (GT * g + r - LAG_L2) % X2_SLOTS * TILE
                        elif r >= LAG_L2:
                            at = (g % 2) * (GT * TILE) + (r - LAG_L2) * TILE
                        else:
                            at = ((g + 1) % 2) * (GT * TILE) + (GT + r - LAG_L2) * TILE
                        nc.vector.tensor_tensor(x2_lo[:, k, :], x2[:, bass.ds(at, TILE)],
                                                x2_hi[:, k, :], ALU.subtract
                                                ).then_inc(s_x2_lo, 1)
                    if live(g, r, LAG_A1):
                        dve.wait_ge(s_a1_hi, done(g, r, LAG_A1))
                        k = (r - LAG_A1) % 2
                        nc.vector.scalar_tensor_tensor(a1_lo[:, k, :], ps_a1[:], 0.0,
                                                       a1_hi[:, k, :], ALU.max, ALU.subtract
                                                       ).then_inc(s_a1_lo, 1)
                    if r % QT == QT - 1:
                        q = (r // QT + 1) % GQ
                        if q and group_live(g, 0):
                            make_onehot(g, q, True)
                        if not q and has_next:
                            make_onehot(g + 1, q, True)
                    if r == R_PX and has_next:
                        user_split(g + 1)
                    if r == R_USER0 and has_next:
                        dve.wait_ge(s_a1, done(g, HT - 1, 0))
                        user_join(g + 1, 0)
                    if r == R_USER1 and group_live(g, 0) and not (isinstance(g, int) and g == 0):
                        dve.wait_ge(s_a1, done(g, 0, 1))
                        user_join(g, 1)
                    if group_live(g, 1):
                        logits = ps_lg[:].rearrange("p (n k) -> p n k", k=DEG)

                        def by_node(col):
                            return col[:].rearrange("p (n a) -> p n a", a=1).broadcast_to(
                                [P, NPT, DEG])

                        def rows(t):
                            return t[:].rearrange("p (n k) -> p n k", k=DEG)

                        if r == R_MAX:
                            dve.wait_ge(s_lg, g * GQ)
                            nc.vector.reduce_max(mx[:], logits, axis=AX.X).then_inc(s_max, 1)
                        if r == R_SUB:
                            dve.wait_ge(s_max, g)
                            nc.vector.tensor_scalar(mxb[:], mx[:], ba3_all[:, 0:1], None, ALU.add
                                                    ).then_inc(s_maxb, 1)
                            dve.wait_ge(s_maxb, g)
                            nc.vector.scalar_tensor_tensor(
                                rows(shifted), logits, ba3_all[:, 0:1], by_node(mxb),
                                ALU.add, ALU.subtract).then_inc(s_sub, 1)
                        if r == R_EXPSUM:
                            dve.wait_ge(s_exp, g)
                            nc.vector.reduce_sum(den[:], rows(expo), axis=AX.X).then_inc(s_den, 1)
                        if r == R_NORM:
                            dve.wait_ge(s_den, g)
                            nc.vector.reciprocal(rden[:], den[:]).then_inc(s_rden, 1)
                            dve.wait_ge(s_rden, g)
                            nc.vector.tensor_tensor(rows(attn), rows(expo), by_node(rden),
                                                    ALU.mult).then_inc(s_attn, 1)
                            dve.wait_ge(s_attn, g)
                            nc.vector.tensor_scalar(attn_s[:], attn[:],
                                                    cst[:, C_SGN + 2:C_SGN + 3], None, ALU.mult
                                                    ).then_inc(s_attn_s, 1)

            groups(dve, group, R_OUT + 1)

        @block.tensor
        def _(pe):
            def product(dst, hi, lo, x_hi, x_lo, more=()):
                terms = [(hi, x_hi), (lo, x_hi), (hi, x_lo), *more]
                for k, (w, x) in enumerate(terms):
                    last = nc.tensor.matmul(dst, w, x, start=k == 0, stop=k == len(terms) - 1)
                return last

            def transpose_user(g):
                pe.wait_ge(s_user, (g + 1) * 16)
                nc.tensor.transpose(ps_ut, user_rows[:], ident).then_inc(s_ut, 1)

            def users(g):
                pe.wait_ge(s_utc, g + 1)
                for half in range(2):
                    cols = user_T[:, HT * half:HT * half + HT, :, :]
                    last = nc.tensor.matmul(ps_uw[:, D * half:D * half + D],
                                            cols.rearrange("p t a j -> p (t a j)"),
                                            wa1_f[:, 1, :], start=True, stop=True)
                last.then_inc(s_uw, 1)

            pe.wait_ge(s_const, 16 * 11)
            pe.wait_ge(s_rrows, 16 * 2 * QT)
            nc.tensor.transpose(ps_m[:, 0:P], rating_rows[:], ident).then_inc(s_rt, 1)
            pe.wait_ge(s_rtc, 1)
            nc.tensor.matmul(ps_m[:, P:2 * P], rating_T[:], w1_f[:, 1, :], start=True,
                             stop=True).then_inc(s_rw, 1)
            pe.wait_ge(s_setup, 1)
            transpose_user(0)
            users(0)

            def group(g, rounds):
                for r in range(rounds):
                    has_next = group_live(g, 0) and group_live(g, -1)
                    if live(g, r, 0):
                        slot = r % GATHER_SLOTS
                        if isinstance(g, int):
                            uses = (GT * g + r) // GATHER_SLOTS + 1
                        else:
                            uses = g * (GT // GATHER_SLOTS) + (r // GATHER_SLOTS + 1)
                        pe.wait_ge(s_gather[slot], uses * (16 * CPT))
                        if live(g, r, 1):
                            pe.wait_ge(s_e_lo, done(g, r, 1))
                        for c in range(CPT):
                            last = nc.tensor.transpose(ps_t[:, P * c:P * c + P],
                                                       gathered[:, slot, c, :], ident)
                        last.then_inc(s_t, 1)
                    elif live(g, r, 1):
                        pe.wait_ge(s_e_lo, done(g, r, 1))
                    if r == R_OUT and group_live(g, 2):
                        pe.wait_ge(s_sum, done(g, r, LAG_SUM + 1))
                        if has_next:
                            pe.wait_ge(s_utc, g + 2)
                        elif group_live(g, 3):
                            pe.wait_ge(s_out_c, g - 2)
                        nc.tensor.transpose(ps_out, out_T[:], ident).then_inc(s_out_t, 1)
                    if live(g, r, LAG_L1):
                        t = (r - LAG_L1) % GT
                        if t % QT == 0:
                            pe.wait_ge(s_onehot, g * GQ + ((r - LAG_L1) // QT + 1))
                        if live(g, r, LAG_L2):
                            pe.wait_ge(s_x1_lo, done(g, r, LAG_L2))
                        product(ps_l1[:], w1_hi[:], w1_lo[:], e_hi[:, t % 2, :], e_lo[:, t % 2, :],
                                [(rating_st[:, t % QT, :], onehot[:, t // QT % 2, :])]
                                ).then_inc(s_l1, 1)
                    elif live(g, r, LAG_L2):
                        pe.wait_ge(s_x1_lo, done(g, r, LAG_L2))
                    if r % QT == 0 and live(g, r, LOGIT_DELAY):
                        pe.wait_ge(s_a2f, done(g, r, LAG_A2 + 1))
                        j = (r - LOGIT_DELAY) // QT % GQ
                        if j == 0 and live(g, r, LOGIT_DELAY + GT):
                            pe.wait_ge(s_sub, g + (r - LOGIT_DELAY) // GT)
                        for q in range(QT):
                            t = (r - LOGIT_DELAY + q) % A2_SLOTS
                            last = nc.tensor.matmul(ps_lg[32 * q:32 * q + 32, :], wa3_cols[:, j, :],
                                                    a2[:, t, :], start=j == 0, stop=j == GQ - 1,
                                                    tile_position=(0, 32 * q))
                        last.then_inc(s_lg, 1)
                    if live(g, r, LAG_L2):
                        k = (r - LAG_L2) % 2
                        if live(g, r, LAG_L2 + 1):
                            pe.wait_ge(s_x2_lo, done(g, r, LAG_L2 + 1))
                        product(ps_l2[:], w2_hi[:], w2_lo[:], x1_hi[:, k, :], x1_lo[:, k, :]
                                ).then_inc(s_l2, 1)
                    elif live(g, r, LAG_A1):
                        pe.wait_ge(s_x2_lo, done(g, r, LAG_A1))
                    if live(g, r, LAG_A1):
                        t = (r - LAG_A1) % GT
                        if t % HT == 0:
                            pe.wait_ge(s_ust, g * 2 + ((r - LAG_A1) // HT + 1))
                        if live(g, r, LAG_A2):
                            pe.wait_ge(s_a1_lo, done(g, r, LAG_A2))
                        product(ps_a1[:], wa1_hi[:], wa1_lo[:], x2_hi[:, t % 2, :],
                                x2_lo[:, t % 2, :],
                                [(user_st[:, t // HT, :], ind[:, t % HT, :])]).then_inc(s_a1, 1)
                    elif live(g, r, LAG_A2):
                        pe.wait_ge(s_a1_lo, done(g, r, LAG_A2))
                    if live(g, r, LAG_A2):
                        k = (r - LAG_A2) % 2
                        if live(g, r, LAG_A2 + 1):
                            pe.wait_ge(s_a2f, done(g, r, LAG_A2 + 1))
                        product(ps_a2[:], wa2_hi[:], wa2_lo[:], a1_hi[:, k, :], a1_lo[:, k, :]
                                ).then_inc(s_a2, 1)
                    if live(g, r, LAG_BC):
                        t = (r - LAG_BC) % GT
                        if t == 0:
                            pe.wait_ge(s_attn_w, g)
                        if live(g, r, LAG_BC + 1):
                            pe.wait_ge(s_mul, done(g, r, LAG_BC + 1))
                        nc.tensor.matmul(ps_bc[:], sel[:, t, :], attn_w[:], start=True, stop=True
                                         ).then_inc(s_bc, 1)
                    if r == R_PT and has_next:
                        if group_live(g, 3):
                            pe.wait_ge(s_out_c, g - 2)
                        pe.wait_ge(s_ux, g + 1)
                        transpose_user(g + 1)
                    if r == R_PW and has_next:
                        if group_live(g, 2):
                            pe.wait_ge(s_out_c, g - 1)
                        users(g + 1)

            groups(pe, group, R_OUT + 1)


def kernel(r_nodes, r_uv_adjacency, r_ratings, L0_rec_user_emb, L0_rec_item_emb, L0_rec_rating_emb,
           L0_rec_w1, L0_rec_b1, L0_rec_w2, L0_rec_b2, L0_rec_wa1, L0_rec_ba1, L0_rec_wa2,
           L0_rec_ba2, L0_rec_wa3, L0_rec_ba3):
    import concourse.bacc as bacc
    from concourse.bass_utils import run_bass_kernel_spmd

    edge_idx = np.ascontiguousarray(
        np.asarray(r_uv_adjacency).reshape(GROUPS, GQ, QT * CPT, P).transpose(0, 1, 3, 2))
    node_idx = np.asarray(r_nodes).reshape(GROUPS, P, 1)
    ratings = np.asarray(r_ratings).reshape(GROUPS, GQ, QT, TILE)
    consts, node_of_edge = constants()
    arrays = {
        "edge_idx": edge_idx, "node_idx": node_idx, "ratings": ratings,
        "user_emb": L0_rec_user_emb, "item_emb": L0_rec_item_emb, "rating_emb": L0_rec_rating_emb,
        "w1": L0_rec_w1, "b1": L0_rec_b1, "w2": L0_rec_w2, "b2": L0_rec_b2,
        "wa1": L0_rec_wa1, "ba1": L0_rec_ba1, "wa2": L0_rec_wa2, "ba2": L0_rec_ba2,
        "wa3": L0_rec_wa3, "ba3": L0_rec_ba3, "consts": consts, "node_of_edge": node_of_edge,
    }
    arrays = {name: np.asarray(a) for name, a in arrays.items()}
    nc = bacc.Bacc("TRN2", target_bir_lowering=False, num_devices=1)
    args = {name: nc.dram_tensor(f"in_{name}", a.shape, mybir.dt.from_np(a.dtype),
                                 kind="ExternalInput").ap() for name, a in arrays.items()}
    out = nc.dram_tensor("out_rows_dram", (GROUPS, GN, D), F32, kind="ExternalOutput").ap()
    build_program(nc, out=out, **args)
    result = run_bass_kernel_spmd(nc, [{f"in_{n}": a for n, a in arrays.items()}], core_ids=[0])
    return result.results[0]["out_rows_dram"].reshape(NODES, D)
```
